# Optimizing a Trainium2 kernel written in Bass

```python
import numpy as np
import jax
import jax.numpy as jnp

def _softmax(x, axis=-1):
    return jax.nn.softmax(x, axis=axis)

def _gelu(x):
    return jax.nn.gelu(x, approximate=True)

def _silu(x):
    return jax.nn.silu(x)

def _sigmoid(x):
    return jax.nn.sigmoid(x)

def _layernorm(x, axis=-1, eps=1e-05):
    m = jnp.mean(x, axis=axis, keepdims=True)
    v = jnp.var(x, axis=axis, keepdims=True)
    return (x - m) / jnp.sqrt(v + eps)

def _scatter_add(tgt, idx, src, axis=0):
    return tgt.at[idx].add(src)

def _segment_sum(src, seg, n):
    return jax.ops.segment_sum(src, seg, n)
kernel_name = 'mk_adj_resnorm_d2_adj_r2_23aab6'

def setup_inputs(seed: int=0):
    np.random.seed(seed)
    _w = jnp.asarray

    def _rec_inputs():
        import jax
        import jax.numpy as jnp
        _gk = jax.random.key(seed)
        x = -0.000929 + 1 * jax.random.normal(jax.random.fold_in(_gk, 1), (8192, 64), jnp.float32)
        _a = jax.random.bernoulli(jax.random.fold_in(_gk, 2), 0.000488281, (8192, 8192))
        _a = jnp.logical_or(_a, jnp.swapaxes(_a, -1, -2))
        _a = jnp.logical_or(_a, jnp.eye(8192, dtype=bool))
        _af = _a.astype(jnp.float32)
        _af = _af * jax.random.uniform(jax.random.fold_in(_gk, 3), (8192, 8192), jnp.float32, 0.05, 1)
        adj = _af
        return (x, adj)
    x, adj = _rec_inputs()

    def _L0_gnn_setup():
        import jax, jax.numpy as jnp
        import numpy as np
        P_DROP = 0.1
        key = jax.random.key(seed)
        k1, k2, k3 = jax.random.split(key, 3)
        N, D = (8192, 64)
        x = jax.random.normal(k1, (N, D), dtype=jnp.float32)
        adj = jax.random.uniform(k2, (N, N), dtype=jnp.float32)
        u = jax.random.uniform(k3, (N, D), dtype=jnp.float32)
        return {'x': x, 'adj': adj, 'u': u}
    _L0_gnn_all = _L0_gnn_setup()
    _L0_gnn_in = {k: v for k, v in _L0_gnn_all.items() if k in ('u',)}
    del _L0_gnn_all

    def _L1_gnn_setup():
        import jax, jax.numpy as jnp
        import numpy as np
        EPS = 1e-08

        def poincare_expmap(v, c):
            sc = jnp.sqrt(c)
            norm = jnp.linalg.norm(v, axis=-1, keepdims=True)
            norm = jnp.clip(norm, 0.0, 10.0)
            return jnp.tanh(sc * norm) * v / (sc * norm + EPS)

        def poincare_logmap(y, c):
            sc = jnp.sqrt(c)
            norm = jnp.linalg.norm(y, axis=-1, keepdims=True)
            norm = jnp.clip(norm, 0.0, 0.999)
            return jnp.arctanh(sc * norm) * y / (sc * norm + EPS)
        key = jax.random.key(seed)
        k1, k2, k3 = jax.random.split(key, 3)
        N, F, U = (8192, 64, 64)
        x = jax.random.normal(k1, (N, F), dtype=jnp.float32)
        adj = jax.random.uniform(k2, (N, N), dtype=jnp.float32)
        kernel = jax.random.normal(k3, (F, U), dtype=jnp.float32)
        kernel = kernel / (jnp.linalg.norm(kernel, axis=0, keepdims=True) + EPS)
        bias = jnp.zeros((U,), dtype=jnp.float32)
        return {'x': x, 'adj': adj, 'kernel': kernel, 'bias': bias}
    _L1_gnn_all = _L1_gnn_setup()
    _L1_gnn_in = {k: v for k, v in _L1_gnn_all.items() if k in ('kernel', 'bias')}
    del _L1_gnn_all
    return {'x': x, 'adj': adj, 'L0_gnn_u': _L0_gnn_in['u'], 'L1_gnn_kernel': _L1_gnn_in['kernel'], 'L1_gnn_bias': _L1_gnn_in['bias']}

def reference(x, adj, L0_gnn_u, L1_gnn_kernel, L1_gnn_bias):
    import jax
    import jax.numpy as jnp

    def _L0_gnn_ref(x, adj, u):
        import jax, jax.numpy as jnp
        import numpy as np
        P_DROP = 0.1
        keep = (u >= P_DROP).astype(x.dtype)
        x_drop = x * keep / (1.0 - P_DROP)
        return jnp.matmul(adj, x_drop)

    def _L1_gnn_ref(x, adj, kernel, bias):
        import jax, jax.numpy as jnp
        import numpy as np
        EPS = 1e-08

        def poincare_expmap(v, c):
            sc = jnp.sqrt(c)
            norm = jnp.linalg.norm(v, axis=-1, keepdims=True)
            norm = jnp.clip(norm, 0.0, 10.0)
            return jnp.tanh(sc * norm) * v / (sc * norm + EPS)

        def poincare_logmap(y, c):
            sc = jnp.sqrt(c)
            norm = jnp.linalg.norm(y, axis=-1, keepdims=True)
            norm = jnp.clip(norm, 0.0, 0.999)
            return jnp.arctanh(sc * norm) * y / (sc * norm + EPS)
        c = 1.0
        x_proj = poincare_expmap(x, c)
        support = adj @ x_proj
        out = poincare_logmap(support, c)
        return out @ kernel + bias
    x = _layernorm(x + _L0_gnn_ref(x, adj, L0_gnn_u), axis=-1)
    x = _layernorm(x + _L1_gnn_ref(x, adj, L1_gnn_kernel, L1_gnn_bias), axis=-1)
    return x

_drawn_inputs = setup_inputs


def setup_inputs(seed=0):
    import zlib

    import numpy as np

    out = dict(_drawn_inputs(seed))
    spreads = {'L1_gnn_bias': (0.0, 0.1)}
    factors = {}
    for name, (base, spread) in spreads.items():
        noise = np.random.default_rng([zlib.crc32(name.encode()), seed]).standard_normal(out[name].shape)
        drawn = base * np.exp(spread * noise) if base else spread * noise
        out[name] = jnp.asarray(drawn.astype(out[name].dtype))
    for name, factor in factors.items():
        out[name] = (out[name] * factor).astype(out[name].dtype)
    return out
```

```python
from contextlib import ExitStack

import concourse.bass as bass
from concourse import mybir

P = 128
N = 8192
F = 64
BS = 512
NB = N // BS
TB = BS // P
NT = N // P
SLOTS = 16
CHUNK = 8
KEEP_PROB = 1.0 - 0.1
LN_EPS = 1e-5
MAP_EPS = 1e-8
SERIES_BELOW = 0.25

TURN_AFTER = 1
COLUMN_AFTER = 4
FINISH_EVERY = 2

HELD = [6] + [4] * 9 + [5, 5, 4, 3, 2, 1]


def reread_early(r):
    if r < 9:
        return []
    row = r - 9
    return [(row, range(row + HELD[row], r))]


def work_order():
    order = []
    parts = 0
    reread_to = {r: r + HELD[r] for r in range(NB)}

    def partial(row, cols, held):
        nonlocal parts
        cols = list(cols)
        steps = [("part", row, c, parts, c == cols[0], c == cols[-1], held) for c in cols]
        parts += 1
        return steps

    def column(c):
        steps = []
        for row in range(c + 1):
            if c < row + HELD[row]:
                steps += partial(row, [c], True)
        return steps

    for r in range(NB):
        blocks = [("both", r, c) for c in range(r - 1)]
        blocks += [("first", r, c) for c in range(r + HELD[r], NB)]
        if r:
            order += blocks[:TURN_AFTER] + [("turn", r - 1)] + blocks[TURN_AFTER:COLUMN_AFTER]
            order += column(r - 1)
            for row, cols in reread_early(r):
                order += partial(row, cols, False)
                reread_to[row] = r
            order += blocks[COLUMN_AFTER:] + [("both", r, r - 1)]
        else:
            order += blocks
        order += [("hold", r, c) for c in range(r + HELD[r] - 1, r - 1, -1)]

    last = NB - 1
    first_cols = range(reread_to[0], last)
    half = first_cols[:2]
    order += partial(0, half, False) + [("turn", last)]
    order += partial(0, first_cols[2:], False) + column(last)
    reread_to[0] = last
    waiting = [r for r in range(NB) if reread_to[r] >= NB]
    since = 0
    rows = [r for r in range(NB) if reread_to[r] < NB]
    rows.sort(key=lambda r: NB - reread_to[r])
    for row in rows:
        for step in partial(row, range(reread_to[row], NB), False):
            order.append(step)
            since += 1
            if waiting and since >= FINISH_EVERY:
                order.append(("finish", waiting.pop(0)))
                since = 0
        waiting.append(row)
    order += [("finish", r) for r in waiting]
    return order


def place_blocks(order):
    loads, uses, freed, kept = [], {}, [], {}
    times = [0] * SLOTS
    for i, step in enumerate(order):
        kind = step[0]
        if kind in ("turn", "finish"):
            continue
        r, c = step[1:3]
        if kind == "part" and step[6]:
            slot, nth = kept.pop((r, c))
        else:
            n = len(loads)
            assert n < SLOTS or n - SLOTS < len(freed), "every slot is held"
            slot = n if n < SLOTS else freed[n - SLOTS]
            times[slot] += 1
            nth = times[slot]
            loads.append((r, c, slot, max(0, n - SLOTS + 1)))
        if kind == "hold":
            kept[r, c] = slot, nth
        else:
            freed.append(slot)
        uses[i] = slot, nth, len(freed)
    return loads, uses


def build(nc, adj, x, u, selector, weight, bias, out):
    f32 = mybir.dt.float32
    ALU = mybir.AluOpType
    ACT = mybir.ActivationFunctionType

    order = work_order()
    loads, uses = place_blocks(order)
    chunk_order = []
    for _, c, _, _ in loads[:NB]:
        if c * TB // CHUNK not in chunk_order:
            chunk_order.append(c * TB // CHUNK)
    finishes = [s[1] for s in order if s[0] == "finish"]
    last_part = {s[1]: s[3] for s in order if s[0] == "part"}

    def saved_through(r):
        return 1 + 3 * r

    with ExitStack() as es:
        def sb(name, shape):
            return es.enter_context(nc.sbuf_tensor(name, shape, f32))

        def ps(name):
            return es.enter_context(nc.psum_tensor(name, [P, BS], f32))

        def sem(name):
            return es.enter_context(nc.semaphore(name))

        ring = sb("ring", [P, SLOTS, TB, BS])
        feats = sb("feats", [P, NT, 2, F])
        xres = sb("xres", [P, NT, F])
        support = sb("support", [P, NB // 2, BS])
        keep = support[:].rearrange("p a b -> p (a b)").rearrange("p (t f) -> p t f", f=F)
        both_saved = sb("both_saved", [F, BS])
        first_saved = sb("first_saved", [P, BS])
        sel = sb("sel", [P, F])
        selw = sb("selw", [P, 2, F])
        bias_sb = sb("bias_sb", [P, F])
        stats = sb("stats", [P, TB, 6])
        mv = sb("mv", [P, TB, 2])
        base = sb("base", [P, 2, TB])
        power = sb("power", [P, 2, TB])
        rooted = sb("rooted", [P, 2, TB])
        y = sb("y", [P, TB, F])
        square = sb("square", [P, TB, F])
        small = sb("small", [P, 12, TB])
        tanh = sb("tanh", [P, TB])
        logq = sb("logq", [P, TB])

        sums_both = [ps(f"sums_both{i}") for i in range(2)]
        sums_first = [ps(f"sums_first{i}") for i in range(2)]
        sums_part = [ps(f"sums_part{i}") for i in range(2)]
        turned = [ps(f"turned{i}") for i in range(2)]

        block_loaded = [sem(f"block_loaded{i}") for i in range(SLOTS)]
        chunk_loaded = [sem(f"chunk_loaded{i}") for i in range(NT // CHUNK)]
        params_loaded = sem("params_loaded")
        dropped = sem("dropped")
        block_released = sem("block_released")
        row_summed = sem("row_summed")
        row_sums_saved = sem("row_sums_saved")
        row_turned = sem("row_turned")
        row_projected = sem("row_projected")
        turned_read = sem("turned_read")
        part_added = sem("part_added")
        root_asked = sem("root_asked")
        root_ready = sem("root_ready")
        norm_ready = sem("norm_ready")
        tanh_ready = sem("tanh_ready")
        mapped = sem("mapped")
        squared = sem("squared")
        quotient_ready = sem("quotient_ready")
        log_ready = sem("log_ready")
        out_ready = sem("out_ready")
        out_stored = sem("out_stored")
        dve_step = sem("dve_step")

        block = es.enter_context(nc.Block())

        def half(r):
            return slice(F * (r % 2), F * (r % 2) + F)

        @block.sync
        def _(sp):
            seen = set()
            for n, (r, c, slot, released) in enumerate(loads):
                chunk = c * TB // CHUNK
                if r == 0 and n < NB and chunk not in seen:
                    seen.add(chunk)
                    t = slice(chunk * CHUNK, (chunk + 1) * CHUNK)
                    sp.dma_start(xres[:, t, :], x[:, t, :]).then_inc(chunk_loaded[chunk], 16)
                    sp.dma_start(keep[:, t, :], u[:, t, :]).then_inc(chunk_loaded[chunk], 16)
                if released:
                    sp.wait_ge(block_released, released)
                sp.dma_start(ring[:, slot], adj[r, c]).then_inc(block_loaded[slot], 16)

        @block.gpsimd
        def _(pool):
            nc.gpsimd.memset(power[:, 0, :], -0.5).then_inc(root_ready, 1)
            nc.gpsimd.memset(power[:, 1, :], 0.5).then_inc(root_ready, 1)
            pool.wait_ge(root_ready, 2)
            asked = 0
            for step in order:
                if step[0] == "turn":
                    asked += 1
                    pool.wait_ge(root_asked, asked)
                    nc.gpsimd.tensor_tensor(rooted[:], base[:], power[:], ALU.pow).then_inc(root_ready, 1)
                if step[0] == "finish":
                    for which in (1, 0):
                        asked += 1
                        pool.wait_ge(root_asked, asked)
                        nc.gpsimd.tensor_tensor(rooted[:, which, :], base[:, which, :], power[:, which, :],
                                                ALU.pow).then_inc(root_ready, 1)

        @block.scalar
        def _(act):
            act.dma_start(sel[:], selector).then_inc(params_loaded, 16)
            act.dma_start(selw[:, 0, :], selector).then_inc(params_loaded, 16)
            act.dma_start(selw[:, 1, :], weight).then_inc(params_loaded, 16)
            act.dma_start(bias_sb[:], bias).then_inc(params_loaded, 16)

            def store(k):
                r = finishes[k]
                act.wait_ge(out_ready, k + 1)
                act.dma_start(out[:, r * TB:(r + 1) * TB, :], xres[:, r * TB:(r + 1) * TB, :]).then_inc(out_stored, 16)

            finished = 0
            for step in order:
                r = step[1]
                if step[0] == "hold" and step[2] == r:
                    act.wait_ge(row_summed, r + 1)
                    if r:
                        act.wait_ge(row_turned, r)
                        nc.scalar.copy(both_saved[:], sums_both[r % 2][0:F]).then_inc(row_sums_saved, 1)
                        nc.scalar.copy(support[half(r), r // 2], sums_both[r % 2][F:P]).then_inc(row_sums_saved, 1)
                    nc.scalar.copy(first_saved[:], sums_first[r % 2][:]).then_inc(row_sums_saved, 1)
                if step[0] == "turn":
                    act.wait_ge(norm_ready, r + 1)
                    nc.scalar.activation(tanh[:], small[:, 1, :], ACT.Tanh).then_inc(tanh_ready, 1)
                if step[0] == "finish":
                    k, finished = finished, finished + 1
                    act.wait_ge(row_projected, k + 1)
                    if k:
                        act.wait_ge(out_ready, k)
                    bank = turned[(NB + k) % 2][:].rearrange("p (t f) -> p t f", t=TB)
                    nc.scalar.activation(square[:], bank[:, :, 0:F], ACT.Square).then_inc(squared, 1)
                    act.wait_ge(quotient_ready, k + 1)
                    nc.scalar.activation(logq[:], small[:, 4, :], ACT.Ln).then_inc(log_ready, 1)
                    if k:
                        store(k - 1)
            store(NB - 1)
            act.wait_ge(out_stored, 16 * NB)

        @block.vector
        def _(dve):
            V = nc.vector
            steps = [0]

            def done(instruction):
                steps[0] += 1
                instruction.then_inc(dve_step, 1)
                dve.wait_ge(dve_step, steps[0])

            def spread(row):
                return row.unsqueeze(2).broadcast_to([P, TB, F])

            for chunk in chunk_order:
                t = slice(chunk * CHUNK, (chunk + 1) * CHUNK)
                dve.wait_ge(chunk_loaded[chunk], 32)
                done(V.tensor_scalar(keep[:, t, :], keep[:, t, :], 0.1, 1.0 / KEEP_PROB, ALU.is_ge, ALU.mult))
                V.tensor_tensor(feats[:, t, 0, :], xres[:, t, :], keep[:, t, :], ALU.mult).then_inc(dropped, 1)

            def moments():
                for t in range(TB):
                    last = V.bn_stats(stats[:, t, :], y[:, t, :])
                done(last)
                for t in range(TB):
                    last = V.bn_aggr(mv[:, t, :], stats[:, t, :])
                done(last)

            def layer1_end(r):
                tiles = slice(r * TB, (r + 1) * TB)
                dve.wait_ge(row_turned, r + 1)
                bank = turned[r % 2][:, 0:TB * F].rearrange("p (t f) -> p t f", f=F)
                y_done = V.tensor_tensor(y[:], bank, xres[:, tiles, :], ALU.add)
                y_done.then_inc(turned_read, 1)
                dve.wait_ge(turned_read, r + 1)
                moments()
                done(V.tensor_scalar(base[:, 0, :], mv[:, :, 1], LN_EPS, None, ALU.add))
                V.tensor_scalar(base[:, 1, :], mv[:, :, 1], float(F), None, ALU.mult).then_inc(root_asked, 1)
                done(V.tensor_tensor(y[:], y[:], spread(mv[:, :, 0]), ALU.subtract))
                dve.wait_ge(root_ready, 2 + r + 1)
                done(V.tensor_tensor(small[:, 0, :], rooted[:, 0, :], rooted[:, 1, :], ALU.mult))
                V.tensor_scalar(small[:, 1, :], small[:, 0, :], 10.0, None, ALU.min).then_inc(norm_ready, 1)
                dve.wait_ge(norm_ready, r + 1)
                done(V.tensor_scalar(small[:, 2, :], small[:, 1, :], MAP_EPS, None, ALU.add))
                done(V.reciprocal(small[:, 3, :], small[:, 2, :]))
                done(V.tensor_tensor(xres[:, tiles, :], y[:], spread(rooted[:, 0, :]), ALU.mult))
                dve.wait_ge(tanh_ready, r + 1)
                done(V.tensor_tensor(small[:, 2, :], small[:, 3, :], tanh[:], ALU.mult))
                V.tensor_tensor(feats[:, tiles, 1, :], xres[:, tiles, :], spread(small[:, 2, :]),
                                ALU.mult).then_inc(mapped, 1)
                dve.wait_ge(mapped, r + 1)
                if r == 0:
                    dve.wait_ge(params_loaded, 64)
                done(V.tensor_tensor(xres[:, tiles, :], xres[:, tiles, :],
                                     bias_sb[:].unsqueeze(1).broadcast_to([P, TB, F]), ALU.add))

            def add_part(r, n, fresh):
                total, bank = support[half(r), r // 2], sums_part[n % 2]
                if fresh:
                    done(V.tensor_copy(total, bank[0:F]))
                else:
                    done(V.tensor_tensor(total, bank[0:F], total, ALU.add))
                V.tensor_tensor(total, bank[F:P], total, ALU.add).then_inc(part_added, 1)
                dve.wait_ge(part_added, n + 1)

            def layer2_end(r, k):
                tiles = slice(r * TB, (r + 1) * TB)
                roots = 2 + NB + 2 * k
                bank = turned[(NB + k) % 2][:].rearrange("p (t f) -> p t f", t=TB)
                dve.wait_ge(squared, k + 1)
                V.reduce_sum(base[:, 1, :], square[:], axis=mybir.AxisListType.X).then_inc(root_asked, 1)
                dve.wait_ge(root_ready, roots + 1)
                norm, above, below, quotient, sq, series, inv = (small[:, i, :] for i in (1, 2, 3, 4, 5, 6, 7))
                done(V.tensor_scalar(norm, rooted[:, 1, :], 0.999, None, ALU.min))
                done(V.tensor_scalar(below, norm, -1.0, 1.0, ALU.mult, ALU.add))
                done(V.reciprocal(above, below))
                V.scalar_tensor_tensor(quotient, norm, 1.0, above, ALU.add, ALU.mult).then_inc(quotient_ready, 1)
                done(V.tensor_tensor(sq, norm, norm, ALU.mult))
                done(V.tensor_scalar(series, sq, 1.0 / 13, None, ALU.mult))
                for odd in (11, 9, 7, 5, 3):
                    done(V.scalar_tensor_tensor(series, series, 1.0 / odd, sq, ALU.add, ALU.mult))
                done(V.scalar_tensor_tensor(series, series, 1.0, norm, ALU.add, ALU.mult))
                done(V.tensor_scalar(inv, norm, MAP_EPS, None, ALU.add))
                done(V.reciprocal(inv, inv))
                done(V.tensor_scalar(below, norm, SERIES_BELOW, None, ALU.is_lt))
                done(V.tensor_tensor(series, series, below, ALU.mult))
                done(V.tensor_scalar(below, norm, SERIES_BELOW, 0.5, ALU.is_ge, ALU.mult))
                dve.wait_ge(log_ready, k + 1)
                done(V.tensor_tensor(below, below, logq[:], ALU.mult))
                done(V.tensor_tensor(series, series, below, ALU.add))
                done(V.tensor_tensor(series, series, inv, ALU.mult))
                V.tensor_tensor(y[:], bank[:, :, F:2 * F], spread(series), ALU.mult).then_inc(turned_read, 1)
                dve.wait_ge(turned_read, NB + k + 1)
                done(V.tensor_tensor(y[:], y[:], xres[:, tiles, :], ALU.add))
                moments()
                V.tensor_scalar(base[:, 0, :], mv[:, :, 1], LN_EPS, None, ALU.add).then_inc(root_asked, 1)
                done(V.tensor_tensor(y[:], y[:], spread(mv[:, :, 0]), ALU.subtract))
                dve.wait_ge(root_ready, roots + 2)
                V.tensor_tensor(xres[:, tiles, :], y[:], spread(rooted[:, 0, :]), ALU.mult).then_inc(out_ready, 1)

            finished = 0
            touched = set()
            for i, step in enumerate(order):
                if step[0] == "turn":
                    layer1_end(step[1])
                if step[0] == "part" and step[5]:
                    _, r, _, n, _, _, _ = step
                    dve.wait_ge(block_released, uses[i][2])
                    add_part(r, n, r == 0 and r not in touched)
                    touched.add(r)
                if step[0] == "finish":
                    layer2_end(step[1], finished)
                    finished += 1

        @block.tensor
        def _(pe):
            finished = 0

            def two_halves(bank, which, i, start, stop):
                for t in range(TB):
                    at = F * (t % 2)
                    last = nc.tensor.matmul(bank[at:at + F], feats[:, c * TB + t, which, :],
                                            ring[:, uses[i][0], t, :],
                                            start=start and t < 2, stop=stop and t >= TB - 2)
                return last

            for i, step in enumerate(order):
                kind, r = step[:2]
                if i in uses:
                    c = step[2]
                    slot, nth, _ = uses[i]
                    pe.wait_ge(block_loaded[slot], 16 * nth)
                if kind == "both":
                    if c == 0 and r >= 2:
                        pe.wait_ge(row_sums_saved, saved_through(r - 2))
                    pe.wait_ge(mapped, c + 1)
                    for t in range(TB):
                        last = nc.tensor.matmul(sums_both[r % 2][:], feats[:, c * TB + t, :, :],
                                                ring[:, slot, t, :],
                                                start=c == 0 and t == 0, stop=c == r - 1 and t == TB - 1)
                    last.then_inc(block_released, 1)
                if kind in ("first", "hold"):
                    start = c == (r + HELD[r] if r + HELD[r] < NB else NB - 1)
                    if r == 0:
                        pe.wait_ge(dropped, 1 + chunk_order.index(c * TB // CHUNK))
                    if start and r >= 2:
                        pe.wait_ge(row_sums_saved, saved_through(r - 2))
                    last = two_halves(sums_first[r % 2], 0, i, start, kind == "hold" and c == r)
                    if kind == "first":
                        last.then_inc(block_released, 1)
                    elif c == r:
                        last.then_inc(row_summed, 1)
                if kind == "part":
                    _, _, _, n, start, stop, _ = step
                    pe.wait_ge(mapped, c + 1)
                    if start and n >= 2:
                        pe.wait_ge(part_added, n - 1)
                    two_halves(sums_part[n % 2], 1, i, start, stop).then_inc(block_released, 1)
                if kind == "turn":
                    pe.wait_ge(row_sums_saved, saved_through(r))
                    if r == 0:
                        pe.wait_ge(params_loaded, 64)
                    if r >= 2:
                        pe.wait_ge(turned_read, r - 1)
                    for t in range(TB):
                        cols = slice(t * P, (t + 1) * P)
                        to = turned[r % 2][:, t * F:(t + 1) * F]
                        last = nc.tensor.matmul(to, first_saved[:, cols], sel[:], start=True, stop=r == 0)
                        if r:
                            last = nc.tensor.matmul(to, both_saved[:, cols], sel[0:F, :], start=False, stop=True)
                    last.then_inc(row_turned, 1)
                if kind == "finish":
                    pe.wait_ge(part_added, last_part[r] + 1)
                    pe.wait_ge(turned_read, NB + finished - 1)
                    for t in range(TB):
                        last = nc.tensor.matmul(turned[(NB + finished) % 2][:, t * P:(t + 1) * P],
                                                support[half(r), r // 2, t * P:(t + 1) * P],
                                                selw[half(r), :, :], start=True, stop=True)
                    last.then_inc(row_projected, 1)
                    finished += 1


def kernel(x, adj, L0_gnn_u, L1_gnn_kernel, L1_gnn_bias):
    import numpy as np
    import concourse.bacc as bacc
    from concourse.bass_utils import run_bass_kernel_spmd

    def tiled(a):
        return np.ascontiguousarray(np.asarray(a).reshape(NT, P, F).transpose(1, 0, 2))

    blocks = np.asarray(adj).reshape(NB, BS, NB, TB, P).transpose(0, 2, 4, 3, 1)
    arrays = {
        "adj": np.ascontiguousarray(blocks),
        "x": tiled(x),
        "u": tiled(L0_gnn_u),
        "selector": np.concatenate([np.eye(F, dtype=np.float32)] * 2),
        "weight": np.concatenate([np.asarray(L1_gnn_kernel)] * 2),
        "bias": np.ascontiguousarray(np.broadcast_to(np.asarray(L1_gnn_bias), (P, F))),
    }
    nc = bacc.Bacc("TRN2", target_bir_lowering=False, num_devices=1)
    args = [nc.dram_tensor(f"{name}_dram", a.shape, mybir.dt.from_np(a.dtype), kind="ExternalInput").ap()
            for name, a in arrays.items()]
    args.append(nc.dram_tensor("out_dram", (P, NT, F), mybir.dt.float32, kind="ExternalOutput").ap())
    build(nc, *args)
    ran = run_bass_kernel_spmd(nc, [{f"{name}_dram": a for name, a in arrays.items()}], core_ids=[0])
    out = ran.results[0]["out_dram"]
    return np.ascontiguousarray(out.reshape(P, NT, F).transpose(1, 0, 2)).reshape(N, F)
```

```python
from contextlib import ExitStack

import concourse.bass as bass
from concourse import mybir

P = 128
N = 8192
F = 64
BS = 512
NB = N // BS
TB = BS // P
NT = N // P
SLOTS = 17
CHUNK = 8
KEEP_PROB = 1.0 - 0.1
LN_EPS = 1e-5
MAP_EPS = 1e-8
SERIES_BELOW = 0.125

TURN_AFTER = 1
COLUMN_AFTER = 5
FINISH_EVERY = 5
GROUP = 2

HELD = [5, 5, 4, 5, 4, 5, 4, 3, 4, 6, 5, 5, 3, 2, 1, 1]

REREAD = [0, 0, 0, 0, 0, 0, 1, 3, 3, 0, 10, 0, 5, 1, 2, 0]


def work_order():
    order = []
    parts = 0
    reread_to = {r: r + HELD[r] for r in range(NB)}

    def partial(row, cols, held):
        nonlocal parts
        cols = list(cols)
        steps = [("part", row, c, parts, c == cols[0], c == cols[-1], held) for c in cols]
        parts += 1
        return steps

    def column(c):
        steps = []
        for row in range(c + 1):
            if c < row + HELD[row]:
                steps += partial(row, [c], True)
        return steps

    def reread(budget, ready):
        steps = []
        while budget > 0:
            row = min(range(ready), key=lambda q: reread_to[q])
            cols = range(reread_to[row], min(ready, reread_to[row] + budget))
            if not cols:
                break
            steps += partial(row, cols, False)
            reread_to[row] = cols.stop
            budget -= len(cols)
        return steps

    for r in range(NB):
        blocks = [("both", r, c) for c in range(r - 1)]
        blocks += [("first", r, c) for c in range(r + HELD[r], NB)]
        if r:
            order += blocks[:TURN_AFTER] + [("turn", r - 1)] + blocks[TURN_AFTER:COLUMN_AFTER]
            order += column(r - 1)
            order += reread(REREAD[r], r)
            order += blocks[COLUMN_AFTER:] + [("both", r, r - 1)]
        else:
            order += blocks
        order += [("hold", r, c) for c in range(r + HELD[r] - 1, r - 1, -1)]

    last = NB - 1
    order += reread(TURN_AFTER, last) + [("turn", last)]
    order += reread(COLUMN_AFTER - TURN_AFTER, last) + column(last)
    waiting = [r for r in range(NB) if reread_to[r] >= NB]
    since = 0
    rows = [r for r in range(NB) if reread_to[r] < NB]
    rows.sort(key=lambda r: NB - reread_to[r])
    for row in rows:
        for step in partial(row, range(reread_to[row], NB), False):
            order.append(step)
            since += 1
            if since >= FINISH_EVERY and (len(waiting) >= GROUP or (waiting and row == rows[-1])):
                order.append(("finish", tuple(waiting[:GROUP])))
                waiting = waiting[GROUP:]
                since = 0
        waiting.append(row)
    while len(waiting) > 1:
        take = min(GROUP, len(waiting) - 1)
        order.append(("finish", tuple(waiting[:take])))
        waiting = waiting[take:]
    return order + [("finish", tuple(waiting))]


def place_blocks(order):
    loads, uses, freed, kept = [], {}, [], {}
    times = [0] * SLOTS
    for i, step in enumerate(order):
        kind = step[0]
        if kind in ("turn", "finish"):
            continue
        r, c = step[1:3]
        if kind == "part" and step[6]:
            slot, nth = kept.pop((r, c))
        else:
            n = len(loads)
            assert n < SLOTS or n - SLOTS < len(freed), "every slot is held"
            slot = n if n < SLOTS else freed[n - SLOTS]
            times[slot] += 1
            nth = times[slot]
            loads.append((r, c, slot, max(0, n - SLOTS + 1)))
        if kind == "hold":
            kept[r, c] = slot, nth
        else:
            freed.append(slot)
        uses[i] = slot, nth, len(freed)
    return loads, uses


def build(nc, adj, x, u, selector, weight, bias, out):
    f32 = mybir.dt.float32
    ALU = mybir.AluOpType
    ACT = mybir.ActivationFunctionType

    order = work_order()
    loads, uses = place_blocks(order)
    chunk_order = []
    for _, c, _, _ in loads[:NB]:
        if c * TB // CHUNK not in chunk_order:
            chunk_order.append(c * TB // CHUNK)
    groups = [s[1] for s in order if s[0] == "finish"]
    ending = [r for rows in groups for r in rows]
    turn_at = order.index(("turn", NB - 1))
    late = min(s[3] for s in order[turn_at:] if s[0] == "part" and s[4] and s[2] == NB - 1)

    def part_bank(n):
        if n < late:
            return n % 2, n - 2 if n >= 2 else None
        if n < late + 4:
            return ((n % 2, n - 2) if n < late + 2 else (2 + n % 2, None))
        return part_bank(n - 4)[0], n - 4

    last_part = {s[1]: s[3] for s in order if s[0] == "part"}

    def rows_before(k):
        return sum(len(rows) for rows in groups[:k])

    def saved_through(r):
        return 1 + 2 * r

    with ExitStack() as es:
        def sb(name, shape):
            return es.enter_context(nc.sbuf_tensor(name, shape, f32))

        def ps(name):
            return es.enter_context(nc.psum_tensor(name, [P, BS], f32))

        def sem(name):
            return es.enter_context(nc.semaphore(name))

        ring = sb("ring", [P, SLOTS, TB, BS])
        feats = sb("feats", [P, NT, 2, F])
        xres = sb("xres", [P, NT, F])
        support = sb("support", [P, NB // 2, BS])
        keep = support[:].rearrange("p a b -> p (a b)").rearrange("p (t f) -> p t f", f=F)
        row_saved = sb("row_saved", [P, BS])
        square = row_saved[:].rearrange("p (t f) -> p t f", f=F)
        sel = sb("sel", [P, F])
        selw = sb("selw", [P, 2, F])
        bias_sb = sb("bias_sb", [P, F])
        GT = GROUP * TB
        stats = sb("stats", [P, GT, 6])
        mv = sb("mv", [P, GT, 2])
        y = sb("y", [P, GT, F])
        y_of = [y[:], feats[:, 0:GT, 0, :]]
        base, power, rooted = (sb(name, [P, 2, GT]) for name in ("base", "power", "rooted"))
        (norm, below, inverse, quotient, norm_sq, log2n, scale, tanh, logq, minus_mean, shift) = (
            sb(name, [P, GT]) for name in ("norm", "below", "inverse", "quotient", "norm_sq", "log2n",
                                           "scale", "tanh", "logq", "minus_mean", "shift"))
        is_large = es.enter_context(nc.sbuf_tensor("is_large", [P, GT], mybir.dt.uint32))

        sums_both = [ps(f"sums_both{i}") for i in range(2)]
        sums_first = [ps(f"sums_first{i}") for i in range(2)]
        sums_part = [ps(f"sums_part{i}") for i in range(2)]
        turned = [ps(f"turned{i}") for i in range(2)]
        part_banks = sums_part + turned
        projected = [[bank[:].rearrange("p (t f) -> p t f", t=TB) for bank in pair]
                     for pair in (sums_both, sums_first)]

        block_loaded = [sem(f"block_loaded{i}") for i in range(SLOTS)]
        chunk_loaded = [sem(f"chunk_loaded{i}") for i in range(NT // CHUNK)]
        params_loaded = sem("params_loaded")
        dropped = sem("dropped")
        block_released = sem("block_released")
        row_summed = sem("row_summed")
        row_sums_saved = sem("row_sums_saved")
        row_joined = sem("row_joined")
        row_turned = sem("row_turned")
        rows_projected = sem("rows_projected")
        turned_read = sem("turned_read")
        projected_read = sem("projected_read")
        part_added = sem("part_added")
        root_asked = sem("root_asked")
        root_ready = sem("root_ready")
        norm_ready = sem("norm_ready")
        tanh_ready = sem("tanh_ready")
        mapped = sem("mapped")
        squared = sem("squared")
        log_asked = sem("log_asked")
        log_ready = sem("log_ready")
        squares_summed = sem("squares_summed")
        norm_rooted = sem("norm_rooted")
        variance_ready = sem("variance_ready")
        deviation_ready = sem("deviation_ready")
        out_ready = sem("out_ready")
        out_stored = sem("out_stored")
        dve_step = sem("dve_step")

        block = es.enter_context(nc.Block())

        def half(r):
            at = F * (ending.index(r) % 2)
            return slice(at, at + F)

        def total(r):
            return support[half(r), ending.index(r) // 2]

        def spread(row):
            return row.unsqueeze(2).broadcast_to([P, row.shape[1], F])

        @block.sync
        def _(sp):
            seen = set()
            for n, (r, c, slot, released) in enumerate(loads):
                chunk = c * TB // CHUNK
                if r == 0 and n < NB and chunk not in seen:
                    seen.add(chunk)
                    t = slice(chunk * CHUNK, (chunk + 1) * CHUNK)
                    sp.dma_start(xres[:, t, :], x[:, t, :]).then_inc(chunk_loaded[chunk], 16)
                    sp.dma_start(keep[:, t, :], u[:, t, :]).then_inc(chunk_loaded[chunk], 16)
                if released:
                    sp.wait_ge(block_released, released)
                sp.dma_start(ring[:, slot], adj[r, c]).then_inc(block_loaded[slot], 16)

        @block.gpsimd
        def _(pool):
            nc.gpsimd.memset(power[:, 0, :], -0.5).then_inc(root_ready, 1)
            nc.gpsimd.memset(power[:, 1, :], 0.5).then_inc(root_ready, 1)
            pool.wait_ge(root_ready, 2)
            asked = k = 0

            def deviation(k):
                own = slice(0, len(groups[k]) * TB)
                pool.wait_ge(variance_ready, k + 1)
                if k:
                    pool.wait_ge(out_ready, rows_before(k))
                nc.gpsimd.tensor_tensor(rooted[:, 0, own], base[:, 0, own], power[:, 0, own],
                                        ALU.pow).then_inc(deviation_ready, 1)
                pool.wait_ge(deviation_ready, 2 * k + 1)
                nc.gpsimd.tensor_tensor(shift[:, own], minus_mean[:, own], rooted[:, 0, own],
                                        ALU.mult).then_inc(deviation_ready, 1)

            for step in order:
                if step[0] == "turn":
                    asked += 1
                    pool.wait_ge(root_asked, asked)
                    nc.gpsimd.tensor_tensor(rooted[:, :, 0:TB], base[:, :, 0:TB], power[:, :, 0:TB],
                                            ALU.pow).then_inc(root_ready, 1)
                if step[0] == "finish":
                    own = slice(0, len(step[1]) * TB)
                    pool.wait_ge(squares_summed, k + 1)
                    nc.gpsimd.tensor_tensor(rooted[:, 1, own], base[:, 1, own], power[:, 1, own],
                                            ALU.pow).then_inc(norm_rooted, 1)
                    if k:
                        deviation(k - 1)
                    k += 1
            deviation(k - 1)

        @block.scalar
        def _(act):
            act.dma_start(sel[:], selector).then_inc(params_loaded, 16)
            act.dma_start(selw[:, 0, :], selector).then_inc(params_loaded, 16)
            act.dma_start(selw[:, 1, :], weight).then_inc(params_loaded, 16)
            act.dma_start(bias_sb[:], bias).then_inc(params_loaded, 16)

            def normalise(k):
                act.wait_ge(deviation_ready, 2 * (k + 1))
                for g, r in enumerate(groups[k]):
                    for t in range(TB):
                        i = g * TB + t
                        last = nc.scalar.activation(xres[:, r * TB + t, :], y_of[k % 2][:, i, :], ACT.Identity,
                                                    scale=rooted[:, 0, i:i + 1], bias=shift[:, i:i + 1])
                    last.then_inc(out_ready, 1)
                for g, r in enumerate(groups[k]):
                    act.wait_ge(out_ready, rows_before(k) + g + 1)
                    act.dma_start(out[:, r * TB:(r + 1) * TB, :],
                                  xres[:, r * TB:(r + 1) * TB, :]).then_inc(out_stored, 16)

            k = 0
            for step in order:
                r = step[1]
                if step[0] == "hold" and step[2] == r:
                    act.wait_ge(row_summed, r + 1)
                    if r:
                        act.wait_ge(row_turned, r)
                    nc.scalar.copy(row_saved[:], sums_first[r % 2][:]).then_inc(row_sums_saved, 1)
                    if r:
                        nc.scalar.copy(total(r), sums_both[r % 2][F:P]).then_inc(row_sums_saved, 1)
                if step[0] == "turn":
                    act.wait_ge(norm_ready, r + 1)
                    nc.scalar.activation(tanh[:, 0:TB], norm[:, 0:TB], ACT.Tanh).then_inc(tanh_ready, 1)
                if step[0] == "finish":
                    tiles = len(step[1]) * TB
                    act.wait_ge(rows_projected, k + 1)
                    if k:
                        act.wait_ge(squares_summed, k)
                    for g in range(len(step[1])):
                        nc.scalar.activation(square[:, g * TB:(g + 1) * TB, :], projected[k % 2][g][:, :, 0:F],
                                             ACT.Square).then_inc(squared, 1)
                    act.wait_ge(log_asked, k + 1)
                    nc.scalar.activation(logq[:, 0:tiles], quotient[:, 0:tiles], ACT.Ln).then_inc(log_ready, 1)
                    if k:
                        normalise(k - 1)
                    k += 1
            normalise(k - 1)
            act.wait_ge(out_stored, 16 * NB)

        @block.vector
        def _(dve):
            V = nc.vector
            steps = [0]

            def done(instruction):
                steps[0] += 1
                instruction.then_inc(dve_step, 1)
                dve.wait_ge(dve_step, steps[0])

            for chunk in chunk_order:
                t = slice(chunk * CHUNK, (chunk + 1) * CHUNK)
                dve.wait_ge(chunk_loaded[chunk], 32)
                done(V.tensor_scalar(keep[:, t, :], keep[:, t, :], 0.1, 1.0 / KEEP_PROB, ALU.is_ge, ALU.mult))
                V.tensor_tensor(feats[:, t, 0, :], xres[:, t, :], keep[:, t, :], ALU.mult).then_inc(dropped, 1)

            def moments(y, tiles):
                for t in range(tiles):
                    last = V.bn_stats(stats[:, t, :], y[:, t, :])
                done(last)
                for t in range(tiles):
                    last = V.bn_aggr(mv[:, t, :], stats[:, t, :])
                done(last)

            def layer1_join(r):
                dve.wait_ge(row_sums_saved, saved_through(r) - 1)
                V.tensor_tensor(row_saved[0:F], sums_both[r % 2][0:F], row_saved[0:F], ALU.add).then_inc(row_joined, 1)

            def layer1_end(r):
                rows = slice(r * TB, (r + 1) * TB)
                own = slice(0, TB)
                dve.wait_ge(row_turned, r + 1)
                bank = turned[r % 2][:, 0:TB * F].rearrange("p (t f) -> p t f", f=F)
                V.tensor_tensor(y[:, own, :], bank, xres[:, rows, :], ALU.add).then_inc(turned_read, 1)
                dve.wait_ge(turned_read, r + 1)
                moments(y, TB)
                done(V.tensor_scalar(base[:, 0, own], mv[:, own, 1], LN_EPS, None, ALU.add))
                V.tensor_scalar(base[:, 1, own], mv[:, own, 1], float(F), None, ALU.mult).then_inc(root_asked, 1)
                done(V.tensor_tensor(y[:, own, :], y[:, own, :], spread(mv[:, own, 0]), ALU.subtract))
                dve.wait_ge(root_ready, 2 + r + 1)
                done(V.tensor_tensor(below[:, own], rooted[:, 0, own], rooted[:, 1, own], ALU.mult))
                V.tensor_scalar(norm[:, own], below[:, own], 10.0, None, ALU.min).then_inc(norm_ready, 1)
                dve.wait_ge(norm_ready, r + 1)
                done(V.tensor_scalar(below[:, own], norm[:, own], MAP_EPS, None, ALU.add))
                done(V.reciprocal(inverse[:, own], below[:, own]))
                done(V.tensor_tensor(xres[:, rows, :], y[:, own, :], spread(rooted[:, 0, own]), ALU.mult))
                dve.wait_ge(tanh_ready, r + 1)
                done(V.tensor_tensor(scale[:, own], inverse[:, own], tanh[:, own], ALU.mult))
                V.tensor_tensor(feats[:, rows, 1, :], xres[:, rows, :], spread(scale[:, own]),
                                ALU.mult).then_inc(mapped, 1)
                dve.wait_ge(mapped, r + 1)
                if r == 0:
                    dve.wait_ge(params_loaded, 64)
                done(V.tensor_tensor(xres[:, rows, :], xres[:, rows, :],
                                     bias_sb[:].unsqueeze(1).broadcast_to([P, TB, F]), ALU.add))

            def add_part(r, n, fresh):
                sums, bank = total(r), part_banks[part_bank(n)[0]]
                if fresh:
                    done(V.tensor_copy(sums, bank[0:F]))
                else:
                    done(V.tensor_tensor(sums, bank[0:F], sums, ALU.add))
                V.tensor_tensor(sums, bank[F:P], sums, ALU.add).then_inc(part_added, 1)
                dve.wait_ge(part_added, n + 1)

            def square_sums(k):
                own = slice(0, len(groups[k]) * TB)
                dve.wait_ge(squared, rows_before(k + 1))
                V.reduce_sum(base[:, 1, own], square[:, own, :], axis=mybir.AxisListType.X).then_inc(squares_summed, 1)

            def log_scale(k):
                own = slice(0, len(groups[k]) * TB)
                dve.wait_ge(norm_rooted, k + 1)
                done(V.tensor_scalar(norm[:, own], rooted[:, 1, own], 0.999, None, ALU.min))
                done(V.tensor_scalar(below[:, own], norm[:, own], -1.0, 1.0, ALU.mult, ALU.add))
                V.tensor_tensor(norm_sq[:, own], norm[:, own], norm[:, own], ALU.mult)
                done(V.reciprocal(inverse[:, own], below[:, own]))
                V.scalar_tensor_tensor(quotient[:, own], norm[:, own], 1.0, inverse[:, own],
                                       ALU.add, ALU.mult).then_inc(log_asked, 1)
                done(V.tensor_scalar(log2n[:, own], norm_sq[:, own], 2.0 / 7, None, ALU.mult))
                V.tensor_scalar(is_large[:, own], norm[:, own], SERIES_BELOW, None, ALU.is_ge)
                done(V.scalar_tensor_tensor(log2n[:, own], log2n[:, own], 2.0 / 5, norm_sq[:, own], ALU.add, ALU.mult))
                V.tensor_scalar(below[:, own], norm[:, own], 2.0, 2.0 * MAP_EPS, ALU.mult, ALU.add)
                done(V.scalar_tensor_tensor(log2n[:, own], log2n[:, own], 2.0 / 3, norm_sq[:, own], ALU.add, ALU.mult))
                V.reciprocal(scale[:, own], below[:, own])
                done(V.scalar_tensor_tensor(log2n[:, own], log2n[:, own], 2.0, norm[:, own], ALU.add, ALU.mult))
                dve.wait_ge(log_ready, k + 1)
                done(V.copy_predicated(log2n[:, own], is_large[:, own], logq[:, own]))
                done(V.tensor_tensor(scale[:, own], scale[:, own], log2n[:, own], ALU.mult))

            def residual(k):
                tiles = len(groups[k]) * TB
                own = slice(0, tiles)
                yk = y_of[k % 2]
                if k >= 2:
                    dve.wait_ge(out_ready, rows_before(k - 1))
                for g, r in enumerate(groups[k]):
                    for t in range(TB):
                        i = g * TB + t
                        last = V.scalar_tensor_tensor(yk[:, i, :], projected[k % 2][g][:, t, F:2 * F],
                                                      scale[:, i:i + 1], xres[:, r * TB + t, :], ALU.mult, ALU.add)
                last.then_inc(projected_read, 1)
                dve.wait_ge(projected_read, k + 1)
                if k:
                    dve.wait_ge(deviation_ready, 2 * k)
                moments(yk, tiles)
                V.tensor_scalar(base[:, 0, own], mv[:, own, 1], LN_EPS, None, ALU.add)
                V.tensor_scalar(minus_mean[:, own], mv[:, own, 0], -1.0, None, ALU.mult).then_inc(variance_ready, 1)

            k = 0
            touched = set()
            for i, step in enumerate(order):
                if step[0] == "hold" and step[2] == step[1] > 0:
                    layer1_join(step[1])
                if step[0] == "turn":
                    layer1_end(step[1])
                if step[0] == "part" and step[5]:
                    _, r, _, n, _, _, _ = step
                    dve.wait_ge(block_released, uses[i][2])
                    add_part(r, n, r == 0 and r not in touched)
                    touched.add(r)
                if step[0] == "finish":
                    square_sums(k)
                    if k:
                        residual(k - 1)
                    log_scale(k)
                    k += 1
            residual(k - 1)

        @block.tensor
        def _(pe):
            k = 0

            def two_halves(bank, layer, slot, c, start, stop):
                for t in range(TB):
                    at = F * (t % 2)
                    last = nc.tensor.matmul(bank[at:at + F], feats[:, c * TB + t, layer, :],
                                            ring[:, slot, t, :],
                                            start=start and t < 2, stop=stop and t >= TB - 2)
                return last

            for i, step in enumerate(order):
                kind, r = step[:2]
                if i in uses:
                    c = step[2]
                    slot, nth, _ = uses[i]
                    pe.wait_ge(block_loaded[slot], 16 * nth)
                if kind == "both":
                    if c == 0 and r >= 2:
                        pe.wait_ge(row_sums_saved, saved_through(r - 2))
                        if r > 2:
                            pe.wait_ge(row_joined, r - 2)
                    pe.wait_ge(mapped, c + 1)
                    for t in range(TB):
                        last = nc.tensor.matmul(sums_both[r % 2][:], feats[:, c * TB + t, :, :],
                                                ring[:, slot, t, :],
                                                start=c == 0 and t == 0, stop=c == r - 1 and t == TB - 1)
                    last.then_inc(block_released, 1)
                if kind in ("first", "hold"):
                    start = c == (r + HELD[r] if r + HELD[r] < NB else NB - 1)
                    if r == 0:
                        pe.wait_ge(dropped, 1 + chunk_order.index(c * TB // CHUNK))
                    if start and r >= 2:
                        pe.wait_ge(row_sums_saved, saved_through(r - 2))
                    last = two_halves(sums_first[r % 2], 0, slot, c, start, kind == "hold" and c == r)
                    if kind == "first":
                        last.then_inc(block_released, 1)
                    elif c == r:
                        last.then_inc(row_summed, 1)
                if kind == "part":
                    _, _, _, n, start, stop, _ = step
                    pe.wait_ge(mapped, c + 1)
                    bank, before = part_bank(n)
                    if start and before is not None:
                        pe.wait_ge(part_added, before + 1)
                    two_halves(part_banks[bank], 1, slot, c, start, stop).then_inc(block_released, 1)
                if kind == "turn":
                    pe.wait_ge(row_sums_saved, saved_through(r))
                    if r == 0:
                        pe.wait_ge(params_loaded, 64)
                    else:
                        pe.wait_ge(row_joined, r)
                    if r >= 2:
                        pe.wait_ge(turned_read, r - 1)
                    for t in range(TB):
                        last = nc.tensor.matmul(turned[r % 2][:, t * F:(t + 1) * F], row_saved[:, t * P:(t + 1) * P],
                                                sel[:], start=True, stop=True)
                    last.then_inc(row_turned, 1)
                if kind == "finish":
                    rows = r
                    pe.wait_ge(part_added, max(last_part[row] for row in rows) + 1)
                    if k >= 2:
                        pe.wait_ge(projected_read, k - 1)
                    for t in range(TB):
                        for g, row in enumerate(rows):
                            last = nc.tensor.matmul(projected[k % 2][g][:, t, :],
                                                    total(row)[:, t * P:(t + 1) * P],
                                                    selw[half(row), :, :], start=True, stop=True)
                    last.then_inc(rows_projected, 1)
                    k += 1


def kernel(x, adj, L0_gnn_u, L1_gnn_kernel, L1_gnn_bias):
    import numpy as np
    import concourse.bacc as bacc
    from concourse.bass_utils import run_bass_kernel_spmd

    def tiled(a):
        return np.ascontiguousarray(np.asarray(a).reshape(NT, P, F).transpose(1, 0, 2))

    blocks = np.asarray(adj).reshape(NB, BS, NB, TB, P).transpose(0, 2, 4, 3, 1)
    arrays = {
        "adj": np.ascontiguousarray(blocks),
        "x": tiled(x),
        "u": tiled(L0_gnn_u),
        "selector": np.concatenate([np.eye(F, dtype=np.float32)] * 2),
        "weight": np.concatenate([np.asarray(L1_gnn_kernel)] * 2),
        "bias": np.ascontiguousarray(np.broadcast_to(np.asarray(L1_gnn_bias), (P, F))),
    }
    nc = bacc.Bacc("TRN2", target_bir_lowering=False, num_devices=1)
    args = [nc.dram_tensor(f"{name}_dram", a.shape, mybir.dt.from_np(a.dtype), kind="ExternalInput").ap()
            for name, a in arrays.items()]
    args.append(nc.dram_tensor("out_dram", (P, NT, F), mybir.dt.float32, kind="ExternalOutput").ap())
    build(nc, *args)
    ran = run_bass_kernel_spmd(nc, [{f"{name}_dram": a for name, a in arrays.items()}], core_ids=[0])
    out = ran.results[0]["out_dram"]
    return np.ascontiguousarray(out.reshape(P, NT, F).transpose(1, 0, 2)).reshape(N, F)
```
